# Optimizing a Trainium2 kernel written in Bass

```python
import numpy as np
import jax
import jax.numpy as jnp

def _softmax(x, axis=-1):
    return jax.nn.softmax(x, axis=axis)

def _gelu(x):
    return jax.nn.gelu(x, approximate=True)

def _silu(x):
    return jax.nn.silu(x)

def _sigmoid(x):
    return jax.nn.sigmoid(x)

def _layernorm(x, axis=-1, eps=1e-05):
    m = jnp.mean(x, axis=axis, keepdims=True)
    v = jnp.var(x, axis=axis, keepdims=True)
    return (x - m) / jnp.sqrt(v + eps)

def _scatter_add(tgt, idx, src, axis=0):
    return tgt.at[idx].add(src)

def _segment_sum(src, seg, n):
    return jax.ops.segment_sum(src, seg, n)
kernel_name = 'mk_dlrm_tower_d1_rec_r8_49f18b'

def setup_inputs(seed: int=0):
    np.random.seed(seed)
    _w = jnp.asarray

    def _rec_inputs():
        import jax
        import jax.numpy as jnp
        _tk = jax.random.key(seed)
        ids = jnp.stack([jax.random.randint(jax.random.fold_in(_tk, 200 + f), (2048,), 0, v, jnp.int32) for f, v in enumerate([125000, 12500, 1250, 1250, 1250, 1000, 1000, 12500, 12500, 1250, 12500, 1250, 1000, 12500, 1000, 12500, 12500, 1250, 12500, 1250, 1000, 1000, 1250, 1000, 1250, 1250])], axis=1)
        tbl_0 = 0.05 * jax.random.normal(jax.random.fold_in(_tk, 500 + 0), (125000, 128), jnp.float32)
        tbl_1 = 0.05 * jax.random.normal(jax.random.fold_in(_tk, 500 + 1), (12500, 128), jnp.float32)
        tbl_2 = 0.05 * jax.random.normal(jax.random.fold_in(_tk, 500 + 2), (1250, 128), jnp.float32)
        tbl_3 = 0.05 * jax.random.normal(jax.random.fold_in(_tk, 500 + 3), (1250, 128), jnp.float32)
        tbl_4 = 0.05 * jax.random.normal(jax.random.fold_in(_tk, 500 + 4), (1250, 128), jnp.float32)
        tbl_5 = 0.05 * jax.random.normal(jax.random.fold_in(_tk, 500 + 5), (1000, 128), jnp.float32)
        tbl_6 = 0.05 * jax.random.normal(jax.random.fold_in(_tk, 500 + 6), (1000, 128), jnp.float32)
        tbl_7 = 0.05 * jax.random.normal(jax.random.fold_in(_tk, 500 + 7), (12500, 128), jnp.float32)
        tbl_8 = 0.05 * jax.random.normal(jax.random.fold_in(_tk, 500 + 8), (12500, 128), jnp.float32)
        tbl_9 = 0.05 * jax.random.normal(jax.random.fold_in(_tk, 500 + 9), (1250, 128), jnp.float32)
        tbl_10 = 0.05 * jax.random.normal(jax.random.fold_in(_tk, 500 + 10), (12500, 128), jnp.float32)
        tbl_11 = 0.05 * jax.random.normal(jax.random.fold_in(_tk, 500 + 11), (1250, 128), jnp.float32)
        tbl_12 = 0.05 * jax.random.normal(jax.random.fold_in(_tk, 500 + 12), (1000, 128), jnp.float32)
        tbl_13 = 0.05 * jax.random.normal(jax.random.fold_in(_tk, 500 + 13), (12500, 128), jnp.float32)
        tbl_14 = 0.05 * jax.random.normal(jax.random.fold_in(_tk, 500 + 14), (1000, 128), jnp.float32)
        tbl_15 = 0.05 * jax.random.normal(jax.random.fold_in(_tk, 500 + 15), (12500, 128), jnp.float32)
        tbl_16 = 0.05 * jax.random.normal(jax.random.fold_in(_tk, 500 + 16), (12500, 128), jnp.float32)
        tbl_17 = 0.05 * jax.random.normal(jax.random.fold_in(_tk, 500 + 17), (1250, 128), jnp.float32)
        tbl_18 = 0.05 * jax.random.normal(jax.random.fold_in(_tk, 500 + 18), (12500, 128), jnp.float32)
        tbl_19 = 0.05 * jax.random.normal(jax.random.fold_in(_tk, 500 + 19), (1250, 128), jnp.float32)
        tbl_20 = 0.05 * jax.random.normal(jax.random.fold_in(_tk, 500 + 20), (1000, 128), jnp.float32)
        tbl_21 = 0.05 * jax.random.normal(jax.random.fold_in(_tk, 500 + 21), (1000, 128), jnp.float32)
        tbl_22 = 0.05 * jax.random.normal(jax.random.fold_in(_tk, 500 + 22), (1250, 128), jnp.float32)
        tbl_23 = 0.05 * jax.random.normal(jax.random.fold_in(_tk, 500 + 23), (1000, 128), jnp.float32)
        tbl_24 = 0.05 * jax.random.normal(jax.random.fold_in(_tk, 500 + 24), (1250, 128), jnp.float32)
        tbl_25 = 0.05 * jax.random.normal(jax.random.fold_in(_tk, 500 + 25), (1250, 128), jnp.float32)
        _rk = jax.random.fold_in(_tk, 7)
        r_dense_features = -0.000520686 + 1.00062 * jax.random.normal(jax.random.fold_in(_rk, 101), (2048, 128), jnp.float32)
        W_top1 = 0.0405887 * jax.random.normal(jax.random.fold_in(_tk, 801), (607, 512), jnp.float32)
        W_top2 = 0.0441942 * jax.random.normal(jax.random.fold_in(_tk, 802), (512, 256), jnp.float32)
        W_top3 = 0.0625 * jax.random.normal(jax.random.fold_in(_tk, 803), (256, 1), jnp.float32)
        b_top1 = jnp.zeros((512,), jnp.float32)
        b_top2 = jnp.zeros((256,), jnp.float32)
        return (r_dense_features, ids, tbl_0, tbl_1, tbl_2, tbl_3, tbl_4, tbl_5, tbl_6, tbl_7, tbl_8, tbl_9, tbl_10, tbl_11, tbl_12, tbl_13, tbl_14, tbl_15, tbl_16, tbl_17, tbl_18, tbl_19, tbl_20, tbl_21, tbl_22, tbl_23, tbl_24, tbl_25, W_top1, b_top1, W_top2, b_top2, W_top3)
    r_dense_features, ids, tbl_0, tbl_1, tbl_2, tbl_3, tbl_4, tbl_5, tbl_6, tbl_7, tbl_8, tbl_9, tbl_10, tbl_11, tbl_12, tbl_13, tbl_14, tbl_15, tbl_16, tbl_17, tbl_18, tbl_19, tbl_20, tbl_21, tbl_22, tbl_23, tbl_24, tbl_25, W_top1, b_top1, W_top2, b_top2, W_top3 = _rec_inputs()

    def _L0_rec_setup():
        import jax, jax.numpy as jnp
        import numpy as np
        F = 26
        N = F + 1
        _TRIU_I, _TRIU_J = np.triu_indices(N, k=1)
        key = jax.random.key(seed)
        k1, k2 = jax.random.split(key)
        B, D = (2048, 128)
        dense_features = jax.random.normal(k1, (B, D), dtype=jnp.float32)
        sparse_features = jax.random.normal(k2, (B, F, D), dtype=jnp.float32)
        return {'dense_features': dense_features, 'sparse_features': sparse_features}
    _L0_rec_all = _L0_rec_setup()
    _L0_rec_in = {k: v for k, v in _L0_rec_all.items() if k in ()}
    del _L0_rec_all
    return {'r_dense_features': r_dense_features, 'ids': ids, 'tbl_0': tbl_0, 'tbl_1': tbl_1, 'tbl_2': tbl_2, 'tbl_3': tbl_3, 'tbl_4': tbl_4, 'tbl_5': tbl_5, 'tbl_6': tbl_6, 'tbl_7': tbl_7, 'tbl_8': tbl_8, 'tbl_9': tbl_9, 'tbl_10': tbl_10, 'tbl_11': tbl_11, 'tbl_12': tbl_12, 'tbl_13': tbl_13, 'tbl_14': tbl_14, 'tbl_15': tbl_15, 'tbl_16': tbl_16, 'tbl_17': tbl_17, 'tbl_18': tbl_18, 'tbl_19': tbl_19, 'tbl_20': tbl_20, 'tbl_21': tbl_21, 'tbl_22': tbl_22, 'tbl_23': tbl_23, 'tbl_24': tbl_24, 'tbl_25': tbl_25, 'W_top1': W_top1, 'b_top1': b_top1, 'W_top2': W_top2, 'b_top2': b_top2, 'W_top3': W_top3}

def reference(r_dense_features, ids, tbl_0, tbl_1, tbl_2, tbl_3, tbl_4, tbl_5, tbl_6, tbl_7, tbl_8, tbl_9, tbl_10, tbl_11, tbl_12, tbl_13, tbl_14, tbl_15, tbl_16, tbl_17, tbl_18, tbl_19, tbl_20, tbl_21, tbl_22, tbl_23, tbl_24, tbl_25, W_top1, b_top1, W_top2, b_top2, W_top3):
    import jax
    import jax.numpy as jnp

    def _L0_rec_ref(dense_features, sparse_features):
        import jax, jax.numpy as jnp
        import numpy as np
        F = 26
        N = F + 1
        _TRIU_I, _TRIU_J = np.triu_indices(N, k=1)
        combined = jnp.concatenate([dense_features[:, None, :], sparse_features], axis=1)
        interactions = jnp.einsum('bnd,bmd->bnm', combined, combined)
        interactions_flat = interactions[:, _TRIU_I, _TRIU_J]
        return jnp.concatenate([dense_features, interactions_flat], axis=1)
    e = jnp.stack([tbl_0[ids[:, 0]], tbl_1[ids[:, 1]], tbl_2[ids[:, 2]], tbl_3[ids[:, 3]], tbl_4[ids[:, 4]], tbl_5[ids[:, 5]], tbl_6[ids[:, 6]], tbl_7[ids[:, 7]], tbl_8[ids[:, 8]], tbl_9[ids[:, 9]], tbl_10[ids[:, 10]], tbl_11[ids[:, 11]], tbl_12[ids[:, 12]], tbl_13[ids[:, 13]], tbl_14[ids[:, 14]], tbl_15[ids[:, 15]], tbl_16[ids[:, 16]], tbl_17[ids[:, 17]], tbl_18[ids[:, 18]], tbl_19[ids[:, 19]], tbl_20[ids[:, 20]], tbl_21[ids[:, 21]], tbl_22[ids[:, 22]], tbl_23[ids[:, 23]], tbl_24[ids[:, 24]], tbl_25[ids[:, 25]]], axis=1)
    z = _L0_rec_ref(r_dense_features, e)
    z = z.reshape(z.shape[0], -1)
    h = jnp.concatenate([z, r_dense_features], axis=1)
    h = jnp.maximum(h @ W_top1 + b_top1, 0.0)
    h = jnp.maximum(h @ W_top2 + b_top2, 0.0)
    y = h @ W_top3
    return y

_drawn_inputs = setup_inputs


def setup_inputs(seed=0):
    import zlib

    import numpy as np

    out = dict(_drawn_inputs(seed))
    spreads = {'b_top1': (0.0, 0.1), 'b_top2': (0.0, 0.1)}
    factors = {}
    for name, (base, spread) in spreads.items():
        noise = np.random.default_rng([zlib.crc32(name.encode()), seed]).standard_normal(out[name].shape)
        drawn = base * np.exp(spread * noise) if base else spread * noise
        out[name] = jnp.asarray(drawn.astype(out[name].dtype))
    for name, factor in factors.items():
        out[name] = (out[name] * factor).astype(out[name].dtype)
    return out
```

```python
import concourse.bass as bass
from concourse import mybir
from contextlib import ExitStack

P = 128


def rectangles(n):
    room = -(-n * (n - 1) // 2 // P) * P
    for rows in range(n, 0, -1):
        found, j1, at = [], n, 0
        while j1 > 1:
            for r in range(min(rows, j1 - 1), 0, -1):
                rest = (j1 - r) * (j1 - r - 1) // 2
                left, step = j1 - r - 1, max(r - 1, 1)
                least = (left // step) * step * (step - 1) // 2
                if at + r * (j1 - 1) + rest + least <= room:
                    break
            found.append((j1 - r, j1, at))
            at += r * (j1 - 1)
            j1 -= r
        if at <= room:
            return found, room
    raise ValueError(n)


def dlrm_tower(nc, ids, dense, tables, w_dense, w_pairs, b1, w2, b2, w3, out):
    fp32, int32 = mybir.dt.float32, mybir.dt.int32
    ACT, ALU = mybir.ActivationFunctionType, mybir.AluOpType

    B, D = dense.shape
    F = len(tables)
    N = F + 1
    H1, H2 = w2.shape[1] * P, w2.shape[2]
    M1, M2 = H1 // P, H2 // P
    TILES = B // P
    SIDES = 2
    STEPS = TILES // SIDES
    SB = SIDES * P
    RECTANGLES, PLACES = rectangles(N)
    C = PLACES // P
    Q = 4
    GROUPS = [range(q, min(q + Q, N)) for q in range(0, N, Q)]
    NT = 3
    S = 32

    visits = [(side, q) for side in range(SIDES) for q in range(len(GROUPS))]
    per_bank = [len(range(k, len(visits), NT)) for k in range(NT)]

    def visit(side, q):
        n = side * len(GROUPS) + q
        return n % NT, n // NT

    def on_scalar(q):
        return q % 2 == 0

    ctx = ExitStack()
    with ctx:
        def sb(name, shape, dt=fp32):
            return ctx.enter_context(nc.sbuf_tensor(name, shape, dt))

        def pb(name):
            return ctx.enter_context(nc.psum_tensor(name, [P, 512], fp32))

        def sem(name):
            return ctx.enter_context(nc.semaphore(name))

        idx = [sb(f"idx{s}", [P, F], int32) for s in range(SIDES)]
        rows = [sb(f"rows{s}", [P, N, D]) for s in range(SIDES)]
        featT = [sb(f"featT{s}", [P, P * N + S]) for s in range(SIDES)]
        square = sb("square", [P, N - 1, S])
        pairs = sb("pairs", [P, PLACES])
        pairsT = sb("pairsT", [P, C, SB])
        denseT = sb("denseT", [P, SB])
        hid1 = sb("hid1", [P, M1, SB])
        hid2 = sb("hid2", [P, M2, SB])
        y_row = sb("y_row", [1, B])
        ident = sb("ident", [P, P])
        wd_parts = sb("wd_parts", [P, 2, H1])
        wd = sb("wd", [P, H1])
        wp = sb("wp", [P, C, H1])
        w2s = sb("w2s", [P, M1, H2])
        w3s = sb("w3s", [P, M2])
        b1s = sb("b1s", [P, M1])
        b2s = sb("b2s", [P, M2])

        bankT = [pb(f"bankT{k}") for k in range(NT)]
        gram = ctx.enter_context(nc.psum_tensor("gram", [P, S, S], fp32))
        bankZ = pb("bankZ")
        bankH = [pb(f"bankH{k}") for k in range(2)]

        idx_loaded = [sem(f"idx_loaded{s}") for s in range(SIDES)]
        gathers_begun = sem("gathers_begun")
        dense_loaded = [sem(f"dense_loaded{s}") for s in range(SIDES)]
        rows_loaded = [[sem(f"rows_loaded{s}_{q}") for q in range(len(GROUPS))] for s in range(SIDES)]
        rows_used = [sem(f"rows_used{s}") for s in range(SIDES)]
        bankT_full = [sem(f"bankT_full{k}") for k in range(NT)]
        bankT_free = [sem(f"bankT_free{k}") for k in range(NT)]
        ident_zero = sem("ident_zero")
        ident_ready = sem("ident_ready")
        slack_ready = sem("slack_ready")
        weights_loaded = sem("weights_loaded")
        dense_parts_loaded = sem("dense_parts_loaded")
        wd_ready = sem("wd_ready")
        gram_full = sem("gram_full")
        square_ready = sem("square_ready")
        pairs_ready = sem("pairs_ready")
        bankZ_full = sem("bankZ_full")
        pairsT_ready = sem("pairsT_ready")
        bankH_full = [sem(f"bankH_full{k}") for k in range(2)]
        hid1_ready = sem("hid1_ready")
        hid2_ready = sem("hid2_ready")
        y_taken = sem("y_taken")
        y_stored = sem("y_stored")

        ids_t = ids.rearrange("(t p) f -> t p f", p=P)
        dense_t = dense.rearrange("(t p) d -> t p d", p=P)

        block = ctx.enter_context(nc.Block())

        def by_sample(side):
            return featT[side][:, 0:P * N].rearrange("p (b n) -> p b n", n=N)

        @block.sync
        def _(sp):
            with sp.Fori(0, STEPS) as i:
                for side in range(SIDES):
                    sp.wait_ge(rows_used[side], i + 1)
                    t = i * SIDES + side
                    sp.dma_start(idx[side][:, :], ids_t[bass.ds(t, 1), :, :].rearrange("a p f -> p (a f)"))\
                      .then_inc(idx_loaded[side], 16)
                    sp.dma_start(rows[side][:, 0, :], dense_t[bass.ds(t, 1), :, :].rearrange("a p d -> p (a d)"))\
                      .then_inc(dense_loaded[side], 16)
            sp.wait_ge(y_taken, STEPS + 1)
            sp.dma_start(out.rearrange("b a -> a b"), y_row[:, :]).then_inc(y_stored, 16)
            sp.wait_ge(y_stored, 16)

        @block.gpsimd
        def _(pool):
            nc.gpsimd.memset(ident[:, :], 0.0).then_inc(ident_zero, 1)
            pool.wait_ge(ident_zero, 1)
            nc.gpsimd.affine_select(out=ident[:, :], in_=ident[:, :], compare_op=ALU.not_equal, fill=1.0,
                                    base=0, pattern=[[-1, P]], channel_multiplier=1).then_inc(ident_ready, 1)
            with pool.Fori(0, STEPS) as i:
                for side in range(SIDES):
                    pool.wait_ge(idx_loaded[side], i * 16 + 16)
                    nc.gpsimd.sem_inc(gathers_begun, 1)
                    for q, group in enumerate(GROUPS):
                        for slot in group:
                            if slot:
                                f = slot - 1
                                nc.gpsimd.indirect_dma_start(
                                    rows[side][:, slot, :], None, tables[f][:, :],
                                    bass.IndirectOffsetOnAxis(ap=idx[side][:, f:f + 1], axis=0),
                                ).then_inc(rows_loaded[side][q], 16)

        @block.tensor
        def _(pe):
            for side in range(SIDES):
                nc.tensor.sem_inc(rows_used[side], 1)
            pe.wait_ge(ident_ready, 1)
            pe.wait_ge(slack_ready, SIDES)
            pe.wait_ge(weights_loaded, 5 * 16)
            pe.wait_ge(wd_ready, 1)

            def transpose_group(i, side, q):
                k, before = visit(side, q)
                gathered = len([slot for slot in GROUPS[q] if slot])
                pe.wait_ge(rows_loaded[side][q], (i + 1) * (16 * gathered))
                if q == 0:
                    pe.wait_ge(dense_loaded[side], (i + 1) * 16)
                pe.wait_ge(bankT_free[k], i * per_bank[k] + before + 1)
                for n, slot in enumerate(GROUPS[q]):
                    last = nc.tensor.transpose(bankT[k][:, n * P:(n + 1) * P], rows[side][:, slot, :], ident[:, :])
                last.then_inc(bankT_full[k], 1)

            def products(i, side):
                for k in range(NT):
                    of_bank = [n for n, (s, _) in enumerate(visits) if s <= side and n % NT == k]
                    pe.wait_ge(bankT_free[k], i * per_bank[k] + len(of_bank) + 1)
                x = featT[side]
                for g in range(S):
                    for a in range(P // S):
                        at = (a * S + g) * N
                        last = nc.tensor.matmul(gram[a * S:(a + 1) * S, g, 0:N - 1], x[:, at:at + S],
                                                x[:, at + 1:at + N], start=True, stop=True)
                        if g == a == 0:
                            last.then_inc(rows_used[side], 1)
                last.then_inc(gram_full, 1)

            def transpose_pairs(i, side):
                pe.wait_ge(pairs_ready, i * SIDES + side + 1)
                if side:
                    pe.wait_ge(pairsT_ready, i * SIDES + side)
                for c in range(C):
                    last = nc.tensor.transpose(bankZ[:, c * P:(c + 1) * P], pairs[:, c * P:(c + 1) * P], ident[:, :])
                last.then_inc(bankZ_full, 1)

            def layer1(i, half):
                for m in (2 * half, 2 * half + 1):
                    o = bankH[half][:, (m % 2) * SB:(m % 2 + 1) * SB]
                    w = slice(m * P, (m + 1) * P)
                    nc.tensor.matmul(o, wd[:, w], denseT[:, :], start=True, stop=False)
                    for c in range(C):
                        last = nc.tensor.matmul(o, wp[:, c, w], pairsT[:, c, :], start=False, stop=c == C - 1)
                last.then_inc(bankH_full[half], 1)

            with pe.Fori(0, STEPS) as i:
                for q in range(len(GROUPS)):
                    transpose_group(i, 0, q)
                products(i, 0)
                transpose_group(i, 1, 0)
                transpose_group(i, 1, 1)
                transpose_pairs(i, 0)
                for q in range(2, len(GROUPS)):
                    transpose_group(i, 1, q)
                products(i, 1)
                transpose_pairs(i, 1)
                pe.wait_ge(pairsT_ready, i * SIDES + SIDES)
                layer1(i, 0)
                pe.wait_ge(y_taken, i + 1)
                layer1(i, 1)
                pe.wait_ge(hid1_ready, i * 2 + 2)
                for m in range(M2):
                    for c in range(M1):
                        last = nc.tensor.matmul(bankH[0][:, m * SB:(m + 1) * SB], w2s[:, c, m * P:(m + 1) * P],
                                                hid1[:, c, :], start=c == 0, stop=c == M1 - 1)
                last.then_inc(bankH_full[0], 1)
                pe.wait_ge(hid2_ready, i + 1)
                for c in range(M2):
                    last = nc.tensor.matmul(bankH[1][0:1, 0:SB], w3s[:, c:c + 1], hid2[:, c, :],
                                            start=c == 0, stop=c == M2 - 1)
                last.then_inc(bankH_full[1], 1)

        def copy_out(i, eng, copy, side, q):
            k, before = visit(side, q)
            eng.wait_ge(bankT_full[k], i * per_bank[k] + before + 1)
            group = GROUPS[q]
            src = bankT[k][:, 0:len(group) * P].rearrange("p (n b) -> p n b", b=P)
            dst = by_sample(side)[:, :, group[0]:group[-1] + 1].rearrange("p b n -> p n b")
            copy(dst, src).then_inc(bankT_free[k], 1)

        @block.scalar
        def _(act):
            nc.scalar.sem_inc(y_taken, 1)
            act.dma_start(wd_parts[:, :, :], w_dense).then_inc(dense_parts_loaded, 16)
            for dst, src in ((wp[:, :, :], w_pairs), (w2s[:, :, :], w2), (w3s[:, :], w3),
                             (b1s[:, :], b1), (b2s[:, :], b2)):
                act.dma_start(dst, src).then_inc(weights_loaded, 16)
            act.wait_ge(weights_loaded, 5 * 16)

            def pairs_out(i, side):
                act.wait_ge(bankZ_full, i * SIDES + side + 1)
                nc.scalar.copy(pairsT[:, :, side * P:(side + 1) * P],
                               bankZ[:, 0:C * P].rearrange("p (c b) -> p c b", b=P)).then_inc(pairsT_ready, 1)

            with act.Fori(0, STEPS) as i:
                for side in range(SIDES):
                    for q in range(len(GROUPS)):
                        if on_scalar(q):
                            if q == 0:
                                k, before = visit(side, q)
                                act.wait_ge(bankT_full[k], i * per_bank[k] + before + 1)
                                nc.scalar.copy(denseT[:, side * P:(side + 1) * P], bankT[k][:, 0:P])
                            copy_out(i, act, nc.scalar.copy, side, q)
                        if side == 1 and q == 1:
                            pairs_out(i, 0)
                pairs_out(i, 1)
                for half in range(2):
                    act.wait_ge(bankH_full[half], i * 2 + 1)
                    for m in (2 * half, 2 * half + 1):
                        last = nc.scalar.activation(hid1[:, m, :], bankH[half][:, (m % 2) * SB:(m % 2 + 1) * SB],
                                                    ACT.Relu, bias=b1s[:, m:m + 1])
                    last.then_inc(hid1_ready, 1)
                act.wait_ge(bankH_full[0], i * 2 + 2)
                for m in range(M2):
                    last = nc.scalar.activation(hid2[:, m, :], bankH[0][:, m * SB:(m + 1) * SB],
                                                ACT.Relu, bias=b2s[:, m:m + 1])
                last.then_inc(hid2_ready, 1)
                act.wait_ge(bankH_full[1], i * 2 + 2)
                nc.scalar.copy(y_row[:, bass.ds(i * SB, SB)], bankH[1][0:1, 0:SB]).then_inc(y_taken, 1)

        @block.vector
        def _(dve):
            for k in range(NT):
                nc.vector.sem_inc(bankT_free[k], 1)
            for side in range(SIDES):
                nc.vector.memset(featT[side][:, P * N:P * N + S], 0.0).then_inc(slack_ready, 1)
            dve.wait_ge(dense_parts_loaded, 16)
            nc.vector.tensor_tensor(wd[:, :], wd_parts[:, 0, :], wd_parts[:, 1, :], ALU.add).then_inc(wd_ready, 1)
            with dve.Fori(0, STEPS) as i:
                for side in range(SIDES):
                    for q in range(len(GROUPS)):
                        if not on_scalar(q):
                            copy_out(i, dve, nc.vector.tensor_copy, side, q)
                    dve.wait_ge(gram_full, i * SIDES + side + 1)
                    nc.vector.transpose(square[:, :, :], gram[:, :, 0:N - 1].rearrange("p g j -> p j g"))\
                      .then_inc(square_ready, 1)
                    dve.wait_ge(square_ready, i * SIDES + side + 1)
                    for j0, j1, at in RECTANGLES:
                        width = j1 - 1
                        last = nc.vector.tensor_copy(
                            pairs[:, at:at + (j1 - j0) * width].rearrange("p (j i) -> p j i", i=width),
                            square[:, j0 - 1:j1 - 1, 0:width])
                    last.then_inc(pairs_ready, 1)


_TABLES = [f"tbl_{f}" for f in range(26)]


def kernel(**inputs):
    import numpy as _np
    import concourse.bacc as _bacc
    from concourse import mybir as _mybir
    from concourse.bass_utils import run_bass_kernel_spmd as _run

    dense, ids = _np.asarray(inputs["r_dense_features"]), _np.asarray(inputs["ids"])
    w1, w2, w3 = (_np.asarray(inputs[n]) for n in ("W_top1", "W_top2", "W_top3"))
    d, n, h1, h2 = dense.shape[1], ids.shape[1] + 1, w1.shape[1], w2.shape[1]

    found, places = rectangles(n)
    w_pairs = _np.zeros((places, h1), w1.dtype)
    row = {}
    for i in range(n):
        for j in range(i + 1, n):
            row[i, j] = d + len(row)
    for j0, j1, at in found:
        for j in range(j0, j1):
            for i in range(j):
                w_pairs[at + (j - j0) * (j1 - 1) + i] = w1[row[i, j]]
    w_pairs = w_pairs.reshape(-1, P, h1).transpose(1, 0, 2)
    w_dense = _np.stack([w1[0:d], w1[d + len(row):]], axis=1)

    arrays = {
        "ids": ids, "dense": dense, **{t: _np.asarray(inputs[t]) for t in _TABLES},
        "w_dense": w_dense, "w_pairs": w_pairs,
        "b1": _np.asarray(inputs["b_top1"]).reshape(-1, P).T,
        "w2": w2.reshape(-1, P, h2).transpose(1, 0, 2),
        "b2": _np.asarray(inputs["b_top2"]).reshape(-1, P).T,
        "w3": w3.reshape(-1, P).T,
    }
    nc = _bacc.Bacc("TRN2", target_bir_lowering=False, num_devices=1)
    given = {k: _np.ascontiguousarray(a) for k, a in arrays.items()}
    ap = {k: nc.dram_tensor(f"in_{k}", a.shape, _mybir.dt.from_np(a.dtype), kind="ExternalInput").ap()
          for k, a in given.items()}
    out = nc.dram_tensor("out_y", (dense.shape[0], 1), _mybir.dt.float32, kind="ExternalOutput").ap()
    dlrm_tower(nc, ap["ids"], ap["dense"], [ap[t] for t in _TABLES], ap["w_dense"], ap["w_pairs"],
               ap["b1"], ap["w2"], ap["b2"], ap["w3"], out)
    r = _run(nc, [{f"in_{k}": a for k, a in given.items()}], core_ids=[0])
    return r.results[0]["out_y"]
```

```python
import concourse.bass as bass
from concourse import mybir
from contextlib import ExitStack

P = 128


def rectangles(n):
    room = -(-n * (n - 1) // 2 // P) * P
    for rows in range(n, 0, -1):
        found, j1, at = [], n, 0
        while j1 > 1:
            for r in range(min(rows, j1 - 1), 0, -1):
                rest = (j1 - r) * (j1 - r - 1) // 2
                left, step = j1 - r - 1, max(r - 1, 1)
                least = (left // step) * step * (step - 1) // 2
                if at + r * (j1 - 1) + rest + least <= room:
                    break
            found.append((j1 - r, j1, at))
            at += r * (j1 - 1)
            j1 -= r
        if at <= room:
            return found, room
    raise ValueError(n)


def chunk_rows(n_rows):
    return max(r for r in range(1, P + 1) if n_rows % r == 0)


def dlrm_tower(nc, cold_ids, hot_ids, dense, cold, hot, w_dense, w_pairs, b1, w2, b2, w3, out):
    fp32, fp32r, int32 = mybir.dt.float32, mybir.dt.float32r, mybir.dt.int32
    ACT, ALU = mybir.ActivationFunctionType, mybir.AluOpType

    B, D = dense.shape
    HOT = len(hot)
    N = 1 + len(cold) + HOT
    NC = 1 + len(cold)
    H1, H2 = w2.shape[1] * P, w2.shape[2]
    M1, M2 = H1 // P, H2 // P
    TILES = B // P
    SIDES = 2
    STEPS = TILES // SIDES
    SB = SIDES * P
    RECTANGLES, PLACES = rectangles(N)
    C = PLACES // P
    Q = 4
    GROUPS = [range(q, min(q + Q, NC)) for q in range(0, NC, Q)]
    S = 32

    R = chunk_rows(hot[0].shape[0])
    CH = [t.shape[0] // R for t in hot]
    assert all(t.shape[0] % R == 0 for t in hot)
    AHEAD = 2
    NSTAGE = 3
    OH = 3
    PER_VISIT = 512 // SB
    LOTS = [range(h, min(h + PER_VISIT, HOT)) for h in range(0, HOT, PER_VISIT)]

    NT = 3
    VISITS = [("T", side, q) for side in range(SIDES) for q in range(len(GROUPS))] \
        + [("hot", 0, m) for m in range(len(LOTS))]
    per_step = [len(range(k, len(VISITS), NT)) for k in range(NT)]
    before_loop = [0] * NT
    for n in range(len(VISITS) - len(LOTS), len(VISITS)):
        before_loop[n % NT] += 1

    def visit(i, what, side, q):
        n = VISITS.index((what, side, q))
        return n % NT, i * per_step[n % NT] + (before_loop[n % NT] + n // NT)

    def filled(i, side, q):
        n = VISITS.index(("T", side, q))
        return n % NT, i * len(range(n % NT, SIDES * len(GROUPS), NT)) + (n // NT + 1)

    def on_scalar(side, q):
        return side == 1 or q % 2 == 0

    BOTH, FIRST, SECOND = slice(0, SB), slice(0, P), slice(P, SB)

    ctx = ExitStack()
    with ctx:
        def sb(name, shape, dt=fp32):
            return ctx.enter_context(nc.sbuf_tensor(name, shape, dt))

        def pb(name):
            return ctx.enter_context(nc.psum_tensor(name, [P, 512], fp32))

        def sem(name):
            return ctx.enter_context(nc.semaphore(name))

        idx = [sb(f"idx{s}", [P, NC - 1], int32) for s in range(SIDES)]
        rows = [sb(f"rows{s}", [P, NC, D]) for s in range(SIDES)]
        featT = [sb(f"featT{s}", [P, P * N + S]) for s in range(SIDES)]
        square = sb("square", [P, N - 1, S])
        pairs = sb("pairs", [P, PLACES])
        pairsT = [sb(f"pairsT_{x}", [P, C, SB], fp32r) for x in ("high", "low")]
        denseT = [sb(f"denseT_{x}", [P, SB], fp32r) for x in ("high", "low")]
        hid1 = sb("hid1", [P, M1, SB])
        hid2 = sb("hid2", [P, M2, SB])
        y_row = sb("y_row", [1, B])
        ident = sb("ident", [P, P])
        row_no_int = sb("row_no_int", [P, max(CH)], int32)
        row_no = sb("row_no", [P, max(CH)])
        ids_wide = sb("ids_wide", [P, HOT, SB], int32)
        onehot = [sb(f"onehot{o}", [P, max(CH), SB], fp32r) for o in range(OH)]
        table = [[sb(f"table{h}_{x}", [P, CH[h], D], fp32r) for x in ("high", "low")] for h in range(HOT)]
        wd = [sb(f"wd_{x}", [P, H1], fp32r) for x in ("high", "low")]
        wp = [sb(f"wp_{x}", [P, C, H1], fp32r) for x in ("high", "low")]
        STAGE = max(2 * H1, max(CH) * D)
        stage = [sb(f"stage{s}", [P, STAGE]) for s in range(NSTAGE)]
        wd_sum = sb("wd_sum", [P, H1])
        w2s = sb("w2s", [P, M1, H2])
        w3s = sb("w3s", [P, M2])
        b1s = sb("b1s", [P, M1])
        b2s = sb("b2s", [P, M2])

        bankT = [pb(f"bankT{k}") for k in range(NT)]
        gram = ctx.enter_context(nc.psum_tensor("gram", [P, S, S], fp32))
        bankZ = pb("bankZ")
        bankH = [pb(f"bankH{k}") for k in range(2)]

        idx_loaded = [sem(f"idx_loaded{s}") for s in range(SIDES)]
        gathers_begun = sem("gathers_begun")
        dense_loaded = [sem(f"dense_loaded{s}") for s in range(SIDES)]
        rows_loaded = [[sem(f"rows_loaded{s}_{q}") for q in range(len(GROUPS))] for s in range(SIDES)]
        rows_used = [sem(f"rows_used{s}") for s in range(SIDES)]
        bankT_full = [sem(f"bankT_full{k}") for k in range(NT)]
        bankT_free = [sem(f"bankT_free{k}") for k in range(NT)]
        ident_zero = sem("ident_zero")
        ident_ready = sem("ident_ready")
        row_no_counted = sem("row_no_counted")
        row_no_ready = sem("row_no_ready")
        slack_ready = sem("slack_ready")
        small_loaded = sem("small_loaded")
        staged = [sem(f"staged{s}") for s in range(NSTAGE)]
        wd_summed = sem("wd_summed")
        high_ready = sem("high_ready")
        split_ready = sem("split_ready")
        ids_wide_loaded = sem("ids_wide_loaded")
        onehot_ready = sem("onehot_ready")
        onehot_used = sem("onehot_used")
        gram_full = sem("gram_full")
        square_ready = sem("square_ready")
        pairs_ready = sem("pairs_ready")
        bankZ_full = sem("bankZ_full")
        pairsT_high_ready = sem("pairsT_high_ready")
        pairsT_ready = sem("pairsT_ready")
        dense_high_ready = sem("dense_high_ready")
        denseT_ready = sem("denseT_ready")
        bankH_full = [sem(f"bankH_full{k}") for k in range(2)]
        hid1_ready = sem("hid1_ready")
        hid2_ready = sem("hid2_ready")
        y_taken = sem("y_taken")
        y_stored = sem("y_stored")

        ids_t = cold_ids.rearrange("(t p) f -> t p f", p=P)
        dense_t = dense.rearrange("(t p) d -> t p d", p=P)

        def staged_view(n, parts, width):
            return stage[n % NSTAGE][0:parts, 0:width]

        SPLITS = []
        for h in range(HOT):
            SPLITS.append((hot[h].rearrange("(c p) d -> p c d", p=R),
                           staged_view(len(SPLITS), R, CH[h] * D).rearrange("p (c d) -> p c d", d=D),
                           [table[h][x][0:R, :, :] for x in range(2)]))
        TABLES_SPLIT = len(SPLITS)
        for c in range(0, C, 2):
            m = min(2, C - c)
            SPLITS.append((w_pairs[:, c:c + m, :],
                           staged_view(len(SPLITS), P, m * H1).rearrange("p (c h) -> p c h", h=H1),
                           [wp[x][:, c:c + m, :] for x in range(2)]))
        DENSE_STAGE = len(SPLITS)
        dense_parts = stage[DENSE_STAGE % NSTAGE][:, 0:2 * H1].rearrange("p (a h) -> p a h", a=2)

        block = ctx.enter_context(nc.Block())

        def by_sample(side):
            return featT[side][:, 0:P * N].rearrange("p (b n) -> p b n", n=N)

        def wait(eng, semaphore, value):
            if not isinstance(value, int) or value > 0:
                eng.wait_ge(semaphore, value)

        @block.sync
        def _(sp):
            def load_tile(i, side):
                t = i * SIDES + side
                sp.dma_start(idx[side][:, :], ids_t[bass.ds(t, 1), :, :].rearrange("a p f -> p (a f)"))\
                  .then_inc(idx_loaded[side], 16)
                sp.dma_start(rows[side][:, 0, :], dense_t[bass.ds(t, 1), :, :].rearrange("a p d -> p (a d)"))\
                  .then_inc(dense_loaded[side], 16)

            def load_ids_wide(i):
                sp.dma_start(ids_wide[:, :, :], hot_ids[:, bass.ds(i * SB, SB)].partition_broadcast(P))\
                  .then_inc(ids_wide_loaded, 16)

            load_tile(0, 0)
            load_ids_wide(0)
            for n in range(DENSE_STAGE + 1):
                wait(sp, split_ready, n - NSTAGE + 1)
                view, src = (SPLITS[n][1], SPLITS[n][0]) if n < DENSE_STAGE else (dense_parts, w_dense)
                sp.dma_start(view, src).then_inc(staged[n % NSTAGE], 16)
                if n == NSTAGE - 1:
                    load_tile(0, 1)
            with sp.Fori(0, STEPS - 1) as i:
                sp.wait_ge(onehot_ready, (i + 1) * HOT)
                load_ids_wide(i + 1)
                for side in range(SIDES):
                    sp.wait_ge(rows_used[side], i + 1)
                    load_tile(i + 1, side)
            sp.wait_ge(y_taken, STEPS + 2)
            sp.dma_start(out.rearrange("b a -> a b"), y_row[:, :]).then_inc(y_stored, 16)
            sp.wait_ge(y_stored, 16)

        @block.gpsimd
        def _(pool):
            nc.gpsimd.memset(ident[:, :], 0.0).then_inc(ident_zero, 1)
            nc.gpsimd.iota(row_no_int[:, :], [[R, max(CH)]], base=0, channel_multiplier=1).then_inc(row_no_counted, 1)
            pool.wait_ge(ident_zero, 1)
            nc.gpsimd.affine_select(out=ident[:, :], in_=ident[:, :], compare_op=ALU.not_equal, fill=1.0,
                                    base=0, pattern=[[-1, P]], channel_multiplier=1).then_inc(ident_ready, 1)
            with pool.Fori(0, STEPS) as i:
                for side in range(SIDES):
                    pool.wait_ge(idx_loaded[side], i * 16 + 16)
                    nc.gpsimd.sem_inc(gathers_begun, 1)
                    for q, group in enumerate(GROUPS):
                        for slot in group:
                            if slot:
                                f = slot - 1
                                nc.gpsimd.indirect_dma_start(
                                    rows[side][:, slot, :], None, cold[f][:, :],
                                    bass.IndirectOffsetOnAxis(ap=idx[side][:, f:f + 1], axis=0),
                                ).then_inc(rows_loaded[side][q], 16)

        @block.tensor
        def _(pe):
            def hot_rows(i, m):
                k, before = visit(i, "hot", 0, m)
                wait(pe, bankT_free[k], before)
                for h in LOTS[m]:
                    pe.wait_ge(onehot_ready, (i + 1) * HOT + (h + 1))
                    o = bankT[k][:, (h - LOTS[m][0]) * SB:(h - LOTS[m][0] + 1) * SB]
                    hot1 = onehot[h % OH]
                    for c in range(CH[h]):
                        for x in range(2):
                            last = nc.tensor.matmul(o, table[h][x][0:R, c, :], hot1[0:R, c, :],
                                                    start=c == x == 0, stop=c == CH[h] - 1 and x == 1)
                    last.then_inc(onehot_used, 1)

            def transpose_group(i, side, q):
                k, before = visit(i, "T", side, q)
                gathered = len([slot for slot in GROUPS[q] if slot])
                pe.wait_ge(rows_loaded[side][q], i * (16 * gathered) + 16 * gathered)
                if q == 0:
                    pe.wait_ge(dense_loaded[side], i * 16 + 16)
                wait(pe, bankT_free[k], before)
                for n, slot in enumerate(GROUPS[q]):
                    last = nc.tensor.transpose(bankT[k][:, n * P:(n + 1) * P], rows[side][:, slot, :], ident[:, :])
                last.then_inc(bankT_full[k], 1)

            def products(i, side):
                upto = VISITS.index(("T", side, len(GROUPS) - 1))
                for k in range(NT):
                    pe.wait_ge(bankT_free[k], i * per_step[k] + (before_loop[k] + len(range(k, upto + 1, NT))))
                x = featT[side]
                for g in range(S):
                    for a in range(P // S):
                        at = (a * S + g) * N
                        last = nc.tensor.matmul(gram[a * S:(a + 1) * S, g, 0:N - 1], x[:, at:at + S],
                                                x[:, at + 1:at + N], start=True, stop=True)
                        if g == a == 0:
                            last.then_inc(rows_used[side], 1)
                last.then_inc(gram_full, 1)

            def transpose_pairs(i, side):
                pe.wait_ge(pairs_ready, i * SIDES + (side + 1))
                if side:
                    pe.wait_ge(pairsT_ready, i * SIDES + side)
                for c in range(C):
                    last = nc.tensor.transpose(bankZ[:, c * P:(c + 1) * P], pairs[:, c * P:(c + 1) * P], ident[:, :])
                last.then_inc(bankZ_full, 1)

            def layer1(n, cols, half):
                if half:
                    pe.wait_ge(y_taken, n + 1)
                for m in (2 * half, 2 * half + 1):
                    w, wide = slice(m * P, (m + 1) * P), cols.stop - cols.start
                    o = bankH[half][:, (m % 2) * wide:(m % 2 + 1) * wide]
                    blocks = [([wd[x][:, w] for x in range(2)], [denseT[x][:, cols] for x in range(2)])]
                    blocks += [([wp[x][:, c, w] for x in range(2)], [pairsT[x][:, c, cols] for x in range(2)])
                               for c in range(C)]
                    for b, (weight, value) in enumerate(blocks):
                        nc.tensor.matmul(o, weight[0], value[0], start=b == 0, stop=False)
                        nc.tensor.matmul(o, weight[0], value[1], start=False, stop=False)
                        last = nc.tensor.matmul(o, weight[1], value[0], start=False, stop=b == C)
                last.then_inc(bankH_full[half], 1)

            def layer2(n, cols):
                pe.wait_ge(hid1_ready, n * 2 + 2)
                wide = cols.stop - cols.start
                for m in range(M2):
                    for c in range(M1):
                        last = nc.tensor.matmul(bankH[0][:, m * wide:(m + 1) * wide], w2s[:, c, m * P:(m + 1) * P],
                                                hid1[:, c, cols], start=c == 0, stop=c == M1 - 1)
                last.then_inc(bankH_full[0], 1)

            def layer3(n, cols):
                pe.wait_ge(hid2_ready, n + 1)
                for c in range(M2):
                    last = nc.tensor.matmul(bankH[1][0:1, 0:cols.stop - cols.start], w3s[:, c:c + 1],
                                            hid2[:, c, cols], start=c == 0, stop=c == M2 - 1)
                last.then_inc(bankH_full[1], 1)

            def step(i, first=False, last=False):
                def second_tile(groups):
                    for q in groups:
                        transpose_group(i, 1, q)

                for q in range(len(GROUPS)):
                    transpose_group(i, 0, q)
                if not first:
                    pe.wait_ge(pairsT_ready, i * SIDES)
                    pe.wait_ge(denseT_ready, i * SIDES)
                    layer1(i - 1, BOTH, 0)
                    layer1(i - 1, BOTH, 1)
                products(i, 0)
                if not last:
                    second_tile(range(len(GROUPS)))
                    transpose_pairs(i, 0)
                if not first:
                    layer2(i - 1, BOTH)
                if last:
                    transpose_pairs(i, 0)
                    layer3(i - 1, BOTH)
                    second_tile(range(len(GROUPS)))
                    pe.wait_ge(pairsT_ready, i * SIDES + 1)
                    pe.wait_ge(denseT_ready, i * SIDES + 1)
                    layer1(i, FIRST, 0)
                    products(i, 1)
                    layer1(i, FIRST, 1)
                    transpose_pairs(i, 1)
                    layer2(i, FIRST)
                    layer3(i, FIRST)
                    return
                products(i, 1)
                if not first:
                    layer3(i - 1, BOTH)
                for m in range(len(LOTS)):
                    if m == 2:
                        transpose_pairs(i, 1)
                    hot_rows(i, m)

            for side in range(SIDES):
                pe.wait_ge(slack_ready, side + 1)
            for m in range(len(LOTS)):
                hot_rows(-1, m)
            pe.wait_ge(ident_ready, 1)
            pe.wait_ge(split_ready, len(SPLITS) + 1)
            pe.wait_ge(small_loaded, 4 * 16)
            step(0, first=True)
            with pe.Fori(1, STEPS - 1) as i:
                step(i)
            step(STEPS - 1, last=True)
            pe.wait_ge(pairsT_ready, STEPS * SIDES)
            pe.wait_ge(denseT_ready, STEPS * SIDES)
            layer1(STEPS, SECOND, 0)
            layer1(STEPS, SECOND, 1)
            layer2(STEPS, SECOND)
            layer3(STEPS, SECOND)

        def copy_group(i, eng, copy, side, q):
            k, count = filled(i, side, q)
            eng.wait_ge(bankT_full[k], count)
            group = GROUPS[q]
            src = bankT[k][:, 0:len(group) * P].rearrange("p (n b) -> p n b", b=P)
            dst = by_sample(side)[:, :, group[0]:group[-1] + 1].rearrange("p b n -> p n b")
            copy(dst, src).then_inc(bankT_free[k], 1)

        @block.scalar
        def _(act):
            nc.scalar.sem_inc(y_taken, 1)
            for dst, src in ((w2s[:, :, :], w2), (w3s[:, :], w3), (b1s[:, :], b1), (b2s[:, :], b2)):
                act.dma_start(dst, src).then_inc(small_loaded, 16)

            def high(n, source, part):
                act.wait_ge(staged[n % NSTAGE], (n // NSTAGE + 1) * 16)
                nc.scalar.copy(part, source).then_inc(high_ready, 1)

            def copy_hot(i, m):
                k, _ = visit(i, "hot", 0, m)
                act.wait_ge(onehot_used, (i + 1) * HOT + (LOTS[m][-1] + 1))
                lot, first = LOTS[m], NC + LOTS[m][0]
                src = bankT[k][:, 0:len(lot) * SB].rearrange("p (n s b) -> p n s b", s=SIDES, b=P)
                for side in range(SIDES):
                    last = nc.scalar.copy(by_sample(side)[:, :, first:first + len(lot)].rearrange("p b n -> p n b"),
                                          src[:, :, side, :])
                last.then_inc(bankT_free[k], 1)

            def pairs_high(i, side):
                act.wait_ge(bankZ_full, i * SIDES + (side + 1))
                nc.scalar.copy(pairsT[0][:, :, side * P:(side + 1) * P],
                               bankZ[:, 0:C * P].rearrange("p (c b) -> p c b", b=P)).then_inc(pairsT_high_ready, 1)

            def hidden1(n, cols):
                wide = cols.stop - cols.start
                for half in range(2):
                    act.wait_ge(bankH_full[half], n * 2 + 1)
                    for m in (2 * half, 2 * half + 1):
                        last = nc.scalar.activation(hid1[:, m, cols], bankH[half][:, (m % 2) * wide:(m % 2 + 1) * wide],
                                                    ACT.Relu, bias=b1s[:, m:m + 1])
                    last.then_inc(hid1_ready, 1)

            def hidden2(n, cols):
                wide = cols.stop - cols.start
                act.wait_ge(bankH_full[0], n * 2 + 2)
                for m in range(M2):
                    last = nc.scalar.activation(hid2[:, m, cols], bankH[0][:, m * wide:(m + 1) * wide],
                                                ACT.Relu, bias=b2s[:, m:m + 1])
                last.then_inc(hid2_ready, 1)

            def result(n, start, wide):
                act.wait_ge(bankH_full[1], n * 2 + 2)
                nc.scalar.copy(y_row[:, bass.ds(start, wide)], bankH[1][0:1, 0:wide]).then_inc(y_taken, 1)

            def step(i, first=False, last=False):
                def copy_groups(side, groups):
                    for q in groups:
                        if on_scalar(side, q):
                            copy_group(i, act, nc.scalar.copy, side, q)

                copy_groups(0, range(len(GROUPS)))
                if not first:
                    hidden1(i - 1, BOTH)
                if not last:
                    copy_groups(1, range(len(GROUPS)))
                    pairs_high(i, 0)
                if not first:
                    hidden2(i - 1, BOTH)
                if last:
                    pairs_high(i, 0)
                    result(i - 1, (i - 1) * SB, SB)
                    copy_groups(1, range(len(GROUPS)))
                    hidden1(i, FIRST)
                    pairs_high(i, 1)
                    hidden2(i, FIRST)
                    result(i, i * SB, P)
                    return
                if not first:
                    result(i - 1, (i - 1) * SB, SB)
                for m in range(len(LOTS)):
                    if m == 2:
                        pairs_high(i, 1)
                    copy_hot(i, m)

            for h in range(HOT):
                high(h, SPLITS[h][1], SPLITS[h][2][0])
                if h >= AHEAD and (h - AHEAD) % PER_VISIT == PER_VISIT - 1:
                    copy_hot(-1, (h - AHEAD) // PER_VISIT)
                    copied = (h - AHEAD) // PER_VISIT + 1
            for m in range(copied, len(LOTS)):
                copy_hot(-1, m)
            for n, (_, view, parts) in enumerate(SPLITS[TABLES_SPLIT:], TABLES_SPLIT):
                high(n, view, parts[0])
            act.wait_ge(wd_summed, 1)
            nc.scalar.copy(wd[0][:, :], wd_sum[:, :]).then_inc(high_ready, 1)
            act.wait_ge(small_loaded, 4 * 16)
            step(0, first=True)
            with act.Fori(1, STEPS - 1) as i:
                step(i)
            step(STEPS - 1, last=True)
            hidden1(STEPS, SECOND)
            hidden2(STEPS, SECOND)
            result(STEPS, STEPS * SB - P, P)

        @block.vector
        def _(dve):
            def low(n, source, parts):
                dve.wait_ge(high_ready, n + 1)
                nc.vector.tensor_tensor(parts[1], source, parts[0].bitcast(fp32), ALU.subtract)\
                  .then_inc(split_ready, 1)

            def onehots(i, h):
                if h == 0:
                    dve.wait_ge(ids_wide_loaded, i * 16 + 32)
                wait(dve, onehot_used, (i + 1) * HOT + (h - OH + 1))
                for c in range(CH[h]):
                    last = nc.vector.tensor_scalar(onehot[h % OH][0:R, c, :], ids_wide[0:R, h, :],
                                                   row_no[0:R, c:c + 1], None, ALU.is_equal)
                last.then_inc(onehot_ready, 1)

            def dense_parts_of(i, side):
                k, before = visit(i, "T", side, 0)
                dve.wait_ge(bankT_free[k], before + 1)
                source, mine = by_sample(side)[:, :, 0], slice(side * P, (side + 1) * P)
                nc.vector.tensor_copy(denseT[0][:, mine], source).then_inc(dense_high_ready, 1)
                dve.wait_ge(dense_high_ready, i * SIDES + (side + 1))
                nc.vector.tensor_tensor(denseT[1][:, mine], source, denseT[0][:, mine].bitcast(fp32),
                                        ALU.subtract).then_inc(denseT_ready, 1)

            def triangle(i, side):
                dve.wait_ge(gram_full, i * SIDES + (side + 1))
                nc.vector.transpose(square[:, :, :], gram[:, :, 0:N - 1].rearrange("p g j -> p j g"))\
                  .then_inc(square_ready, 1)
                dve.wait_ge(square_ready, i * SIDES + (side + 1))
                for j0, j1, at in RECTANGLES:
                    width = j1 - 1
                    last = nc.vector.tensor_copy(
                        pairs[:, at:at + (j1 - j0) * width].rearrange("p (j i) -> p j i", i=width),
                        square[:, j0 - 1:j1 - 1, 0:width])
                last.then_inc(pairs_ready, 1)

            def pairs_low(i, side):
                dve.wait_ge(pairsT_high_ready, i * SIDES + (side + 1))
                mine = slice(side * P, (side + 1) * P)
                nc.vector.tensor_tensor(pairsT[1][:, :, mine], bankZ[:, 0:C * P].rearrange("p (c b) -> p c b", b=P),
                                        pairsT[0][:, :, mine].bitcast(fp32), ALU.subtract).then_inc(pairsT_ready, 1)

            def step(i, last=False):
                def make(*which):
                    if not last:
                        for h in which:
                            onehots(i, h)

                for side in range(SIDES):
                    for q in range(len(GROUPS)):
                        if not on_scalar(side, q):
                            copy_group(i, dve, nc.vector.tensor_copy, side, q)
                    if side == 0:
                        make(*range(OH))
                        triangle(i, 0)
                        pairs_low(i, 0)
                        dense_parts_of(i, 0)
                dense_parts_of(i, 1)
                triangle(i, 1)
                make(*range(OH, HOT))
                pairs_low(i, 1)

            for side in range(SIDES):
                nc.vector.memset(featT[side][:, P * N:P * N + S], 0.0).then_inc(slack_ready, 1)
            dve.wait_ge(row_no_counted, 1)
            nc.vector.tensor_copy(row_no[:, :], row_no_int[:, :]).then_inc(row_no_ready, 1)
            dve.wait_ge(row_no_ready, 1)
            for h in range(HOT):
                _, view, parts = SPLITS[h]
                low(h, view, parts)
                dve.wait_ge(split_ready, h + 1)
                onehots(-1, h)
            for n, (_, view, parts) in enumerate(SPLITS[TABLES_SPLIT:], TABLES_SPLIT):
                low(n, view, parts)
            dve.wait_ge(staged[DENSE_STAGE % NSTAGE], (DENSE_STAGE // NSTAGE + 1) * 16)
            nc.vector.tensor_tensor(wd_sum[:, :], dense_parts[:, 0, :], dense_parts[:, 1, :], ALU.add)\
              .then_inc(wd_summed, 1)
            low(DENSE_STAGE, wd_sum[:, :], [wd[x][:, :] for x in range(2)])
            with dve.Fori(0, STEPS - 1) as i:
                step(i)
            step(STEPS - 1, last=True)


N_TABLES = 26
N_HOT = 7


def kernel(**inputs):
    import numpy as _np
    import concourse.bacc as _bacc
    from concourse import mybir as _mybir
    from concourse.bass_utils import run_bass_kernel_spmd as _run

    dense, ids = _np.asarray(inputs["r_dense_features"]), _np.asarray(inputs["ids"])
    tables = [_np.asarray(inputs[f"tbl_{f}"]) for f in range(N_TABLES)]
    w1, w2, w3 = (_np.asarray(inputs[n]) for n in ("W_top1", "W_top2", "W_top3"))
    d, n, h1, h2 = dense.shape[1], N_TABLES + 1, w1.shape[1], w2.shape[1]

    by_size = sorted(range(N_TABLES), key=lambda f: len(tables[f]))
    hot, cold = sorted(by_size[:N_HOT]), sorted(by_size[N_HOT:])
    feature = [0] + [1 + f for f in cold + hot]

    found, places = rectangles(n)
    w_pairs = _np.zeros((places, h1), w1.dtype)
    row = {}
    for i in range(n):
        for j in range(i + 1, n):
            row[i, j] = d + len(row)
    for j0, j1, at in found:
        for j in range(j0, j1):
            for i in range(j):
                pair = tuple(sorted((feature[i], feature[j])))
                w_pairs[at + (j - j0) * (j1 - 1) + i] = w1[row[pair]]
    w_pairs = w_pairs.reshape(-1, P, h1).transpose(1, 0, 2)
    w_dense = _np.stack([w1[0:d], w1[d + len(row):]], axis=1)

    arrays = {
        "cold_ids": ids[:, cold], "hot_ids": ids[:, hot].T, "dense": dense,
        **{f"tbl_{f}": tables[f] for f in range(N_TABLES)},
        "w_dense": w_dense, "w_pairs": w_pairs,
        "b1": _np.asarray(inputs["b_top1"]).reshape(-1, P).T,
        "w2": w2.reshape(-1, P, h2).transpose(1, 0, 2),
        "b2": _np.asarray(inputs["b_top2"]).reshape(-1, P).T,
        "w3": w3.reshape(-1, P).T,
    }
    nc = _bacc.Bacc("TRN2", target_bir_lowering=False, num_devices=1)
    given = {k: _np.ascontiguousarray(a) for k, a in arrays.items()}
    ap = {k: nc.dram_tensor(f"in_{k}", a.shape, _mybir.dt.from_np(a.dtype), kind="ExternalInput").ap()
          for k, a in given.items()}
    out = nc.dram_tensor("out_y", (dense.shape[0], 1), _mybir.dt.float32, kind="ExternalOutput").ap()
    dlrm_tower(nc, ap["cold_ids"], ap["hot_ids"], ap["dense"], [ap[f"tbl_{f}"] for f in cold],
               [ap[f"tbl_{f}"] for f in hot], ap["w_dense"], ap["w_pairs"],
               ap["b1"], ap["w2"], ap["b2"], ap["w3"], out)
    r = _run(nc, [{f"in_{k}": a for k, a in given.items()}], core_ids=[0])
    return r.results[0]["out_y"]
```

```python
import concourse.bass as bass
from concourse import mybir
from contextlib import ExitStack

P = 128


def rectangles(n):
    room = -(-n * (n - 1) // 2 // P) * P
    for rows in range(n, 0, -1):
        found, j1, at = [], n, 0
        while j1 > 1:
            for r in range(min(rows, j1 - 1), 0, -1):
                rest = (j1 - r) * (j1 - r - 1) // 2
                left, step = j1 - r - 1, max(r - 1, 1)
                least = (left // step) * step * (step - 1) // 2
                if at + r * (j1 - 1) + rest + least <= room:
                    break
            found.append((j1 - r, j1, at))
            at += r * (j1 - 1)
            j1 -= r
        if at <= room:
            return found, room
    raise ValueError(n)


def chunk_rows(n_rows):
    return max(r for r in range(1, P + 1) if n_rows % r == 0)


def dlrm_tower(nc, cold_ids, hot_ids, dense, cold, hot, w_dense, w_pairs, b1, w2, b2, w3, out):
    fp32, fp32r, int32 = mybir.dt.float32, mybir.dt.float32r, mybir.dt.int32
    ACT, ALU = mybir.ActivationFunctionType, mybir.AluOpType

    B, D = dense.shape
    HOT = len(hot)
    N = 1 + len(cold) + HOT
    NC = 1 + len(cold)
    H1, H2 = w2.shape[1] * P, w2.shape[2]
    M1, M2 = H1 // P, H2 // P
    TILES = B // P
    SIDES = 2
    STEPS = TILES // SIDES
    SB = SIDES * P
    RECTANGLES, PLACES = rectangles(N)
    C = PLACES // P
    Q = 4
    GROUPS = [range(q, min(q + Q, NC)) for q in range(0, NC, Q)]
    S = 32

    R = chunk_rows(hot[0].shape[0])
    CH = [t.shape[0] // R for t in hot]
    assert all(t.shape[0] % R == 0 for t in hot)
    AHEAD = 2
    OH = 3
    PER_VISIT = 512 // SB
    OH_CHUNKS = [max(CH[o::OH]) for o in range(OH)]
    LOTS = [range(h, min(h + PER_VISIT, HOT)) for h in range(0, HOT, PER_VISIT)]

    NT = 3
    VISITS = [("T", side, q) for side in range(SIDES) for q in range(len(GROUPS))] \
        + [("hot", 0, m) for m in range(len(LOTS))]
    BANK = [n % NT for n in range(SIDES * len(GROUPS))] \
        + [NT - 1 if m == len(LOTS) - 1 else m % 2 for m in range(len(LOTS))]
    per_step = [BANK.count(k) for k in range(NT)]
    before_loop = [BANK[-len(LOTS):].count(k) for k in range(NT)]

    def visit(i, what, side, q):
        n = VISITS.index((what, side, q))
        k = BANK[n]
        return k, i * per_step[k] + (before_loop[k] + BANK[:n].count(k))

    def filled(i, side, q):
        n = VISITS.index(("T", side, q))
        k = BANK[n]
        return k, i * BANK[:SIDES * len(GROUPS)].count(k) + BANK[:n + 1].count(k)

    def on_scalar(q):
        return q % 2 == 0

    ctx = ExitStack()
    with ctx:
        def sb(name, shape, dt=fp32):
            return ctx.enter_context(nc.sbuf_tensor(name, shape, dt))

        def pb(name):
            return ctx.enter_context(nc.psum_tensor(name, [P, 512], fp32))

        def sem(name):
            return ctx.enter_context(nc.semaphore(name))

        idx = [sb(f"idx{s}", [P, NC - 1], int32) for s in range(SIDES)]
        rows = [sb(f"rows{s}", [P, NC, D]) for s in range(SIDES)]
        featT = [sb(f"featT{s}", [P, P * N + S]) for s in range(SIDES)]
        square_whole = sb("square", [P, S * S])
        square = square_whole[:, 0:(N - 1) * S].rearrange("p (j i) -> p j i", i=S)
        pairs = sb("pairs", [P, PLACES])
        pairsT = [sb(f"pairsT_{x}", [P, C, SB], fp32r) for x in ("high", "low")]
        denseT = [sb(f"denseT_{x}", [P, SB], fp32r) for x in ("high", "low")]
        hid1_whole = sb("hid1_whole", [P, M1, SB])
        hid1 = [sb(f"hid1_{x}", [P, M1, SB], fp32r) for x in ("high", "low")]
        hid2 = sb("hid2", [P, M2, SB])
        ident = sb("ident", [P, P])
        row_no_int = sb("row_no_int", [P, max(CH)], int32)
        row_no = sb("row_no", [P, max(CH)])
        ids_wide = sb("ids_wide", [P, HOT, SB], int32)
        onehot = [sb(f"onehot{o}", [P, OH_CHUNKS[o], SB], fp32r) for o in range(OH)]
        table = [[sb(f"table{h}_{x}", [P, CH[h], D], fp32r) for x in ("high", "low")] for h in range(HOT)]
        wd = [sb(f"wd_{x}", [P, H1], fp32r) for x in ("high", "low")]
        wp = [sb(f"wp_{x}", [P, C, H1], fp32r) for x in ("high", "low")]
        w2s = [sb(f"w2_{x}", [P, M1, H2], fp32r) for x in ("high", "low")]
        w3s = sb("w3s", [P, M2])
        b1s = sb("b1s", [P, M1])
        b2s = sb("b2s", [P, M2])
        TABLE_PLACES = 4
        widths = [max(2 * H1, M1 * H2, max(CH[k::TABLE_PLACES]) * D) for k in range(2)]
        stages = sb("stages", [P, max(sum(widths), B)])
        y_row = stages[0:1, 0:B]
        places = [stages[:, 0:widths[0]], stages[:, widths[0]:sum(widths)],
                  hid1_whole[:, :, :].rearrange("p m b -> p (m b)"), square_whole[:, :], hid2[:, :, :].rearrange("p m b -> p (m b)")]

        bankT = [pb(f"bankT{k}") for k in range(NT)]
        gram = ctx.enter_context(nc.psum_tensor("gram", [P, S, S], fp32))
        bankZ = pb("bankZ")
        bankH = [pb(f"bankH{k}") for k in range(2)]

        idx_loaded = [sem(f"idx_loaded{s}") for s in range(SIDES)]
        gathers_begun = sem("gathers_begun")
        dense_loaded = [sem(f"dense_loaded{s}") for s in range(SIDES)]
        rows_loaded = [[sem(f"rows_loaded{s}_{q}") for q in range(len(GROUPS))] for s in range(SIDES)]
        bankT_full = [sem(f"bankT_full{k}") for k in range(NT)]
        bankT_free = [sem(f"bankT_free{k}") for k in range(NT)]
        ident_zero = sem("ident_zero")
        ident_ready = sem("ident_ready")
        row_no_counted = sem("row_no_counted")
        row_no_ready = sem("row_no_ready")
        slack_ready = sem("slack_ready")
        small_loaded = sem("small_loaded")
        staged = [sem(f"staged{k}") for k in range(len(places))]
        wd_summed = sem("wd_summed")
        high_ready = sem("high_ready")
        split_ready = sem("split_ready")
        first_ids_loaded = sem("first_ids_loaded")
        ids_wide_loaded = sem("ids_wide_loaded")
        onehot_ready = sem("onehot_ready")
        onehot_used = sem("onehot_used")
        gram_full = sem("gram_full")
        square_ready = sem("square_ready")
        pairs_ready = sem("pairs_ready")
        bankZ_full = sem("bankZ_full")
        pairsT_high_ready = sem("pairsT_high_ready")
        pairsT_ready = sem("pairsT_ready")
        dense_high_ready = sem("dense_high_ready")
        denseT_ready = sem("denseT_ready")
        bankH_full = [sem(f"bankH_full{k}") for k in range(2)]
        hid1_full = sem("hid1_full")
        hid1_high_ready = sem("hid1_high_ready")
        hid1_ready = sem("hid1_ready")
        hid2_ready = sem("hid2_ready")
        last1_full = sem("last1_full")
        last1_whole = sem("last1_whole")
        last1_high = sem("last1_high")
        last1_ready = sem("last1_ready")
        last2_full = sem("last2_full")
        last2_ready = sem("last2_ready")
        y_taken = sem("y_taken")
        y_stored = sem("y_stored")

        ids_t = cold_ids.rearrange("(t p) f -> t p f", p=P)
        dense_t = dense.rearrange("(t p) d -> t p d", p=P)

        def tables_part(h):
            cd = CH[h] * D
            return (hot[h].rearrange("(c p) d -> p c d", p=R), h % TABLE_PLACES,
                    places[h % TABLE_PLACES][0:R, 0:cd].rearrange("p (c d) -> p c d", d=D),
                    [table[h][x][0:R, :, :] for x in range(2)])

        def weights_part(source, place, parts, inner):
            blocks = source.shape[1]
            return (source, place, places[place][:, 0:blocks * inner].rearrange("p (c h) -> p c h", h=inner), parts)

        half = (C + 1) // 2
        SPLITS = [tables_part(h) for h in range(HOT)] + [
            weights_part(w_pairs[:, 0:half, :], 0, [wp[x][:, 0:half, :] for x in range(2)], H1),
            weights_part(w_pairs[:, half:C, :], 4, [wp[x][:, half:C, :] for x in range(2)], H1),
            weights_part(w2, 1, [w2s[x][:, :, :] for x in range(2)], H2),
            weights_part(w_dense, 2, [wd[x][:, :] for x in range(2)], H1)]
        WHOLES = len(SPLITS)
        wd_whole = SPLITS[-1][2]

        def user_of_place(n):
            before = [m for m in range(n) if SPLITS[m][1] == SPLITS[n][1]]
            return len(before) + 1, before[-1] if before else None

        block = ctx.enter_context(nc.Block())

        def by_sample(side):
            return featT[side][:, 0:P * N].rearrange("p (b n) -> p b n", n=N)

        def hidden1_at(m):
            return bankH[m // 2][:, (m % 2) * SB:(m % 2 + 1) * SB]

        def last_hidden1_bank(m):
            return (*bankH, *bankT[1:])[m]

        def last_hidden1_at(m):
            return last_hidden1_bank(m)[:, 0:SB]

        def hidden2_at(m):
            return bankH[0][:, m * SB:(m + 1) * SB]

        def last_hidden2_at(m):
            return (bankH[0], bankZ)[m][:, 0:SB]

        def wait(eng, semaphore, value):
            if not isinstance(value, int) or value > 0:
                eng.wait_ge(semaphore, value)

        @block.sync
        def _(sp):
            def load_ids(i, side):
                t = i * SIDES + side
                sp.dma_start(idx[side][:, :], ids_t[bass.ds(t, 1), :, :].rearrange("a p f -> p (a f)"))\
                  .then_inc(idx_loaded[side], 16)

            def load_dense(i, side):
                t = i * SIDES + side
                sp.dma_start(rows[side][:, 0, :], dense_t[bass.ds(t, 1), :, :].rearrange("a p d -> p (a d)"))\
                  .then_inc(dense_loaded[side], 16)

            def load_ids_wide(i):
                sp.dma_start(ids_wide[:, :, :], hot_ids[:, bass.ds(i * SB, SB)].partition_broadcast(P))\
                  .then_inc(ids_wide_loaded, 16)

            def load_whole(n):
                source, place, view, _ = SPLITS[n]
                _, previous = user_of_place(n)
                if previous is not None:
                    sp.wait_ge(split_ready, previous + 1)
                sp.dma_start(view, source).then_inc(staged[place], 16)

            load_ids(0, 0)
            sp.dma_start(ids_wide[:, 0:1, :], hot_ids[0:1, 0:SB].partition_broadcast(P)).then_inc(first_ids_loaded, 16)
            load_whole(0)
            sp.dma_start(ids_wide[:, 1:HOT, :], hot_ids[1:HOT, 0:SB].partition_broadcast(P))\
              .then_inc(ids_wide_loaded, 16)
            load_whole(1)
            load_dense(0, 0)
            load_ids(0, 1)
            load_dense(0, 1)
            for n in range(2, WHOLES):
                load_whole(n)
            for dst, src in ((w3s[:, :], w3), (b1s[:, :], b1), (b2s[:, :], b2)):
                sp.dma_start(dst, src).then_inc(small_loaded, 16)
            with sp.Fori(0, STEPS - 1) as i:
                sp.wait_ge(onehot_ready, (i + 1) * HOT)
                load_ids_wide(i + 1)
                for side in range(SIDES):
                    for q, group in enumerate(GROUPS):
                        gathered = len([slot for slot in group if slot])
                        sp.wait_ge(rows_loaded[side][q], i * (16 * gathered) + 16 * gathered)
                    load_ids(i + 1, side)
                    k, count = filled(i, side, 0)
                    sp.wait_ge(bankT_full[k], count)
                    load_dense(i + 1, side)
            sp.wait_ge(y_taken, STEPS + 1)
            sp.dma_start(out.rearrange("b a -> a b"), y_row[:, :]).then_inc(y_stored, 16)
            sp.wait_ge(y_stored, 16)

        @block.gpsimd
        def _(pool):
            nc.gpsimd.memset(ident[:, :], 0.0).then_inc(ident_zero, 1)
            nc.gpsimd.iota(row_no_int[:, :], [[R, max(CH)]], base=0, channel_multiplier=1).then_inc(row_no_counted, 1)
            pool.wait_ge(ident_zero, 1)
            nc.gpsimd.affine_select(out=ident[:, :], in_=ident[:, :], compare_op=ALU.not_equal, fill=1.0,
                                    base=0, pattern=[[-1, P]], channel_multiplier=1).then_inc(ident_ready, 1)

            def gather(i, side):
                for q, group in enumerate(GROUPS):
                    for slot in group:
                        if slot:
                            f = slot - 1
                            nc.gpsimd.indirect_dma_start(
                                rows[side][:, slot, :], None, cold[f][:, :],
                                bass.IndirectOffsetOnAxis(ap=idx[side][:, f:f + 1], axis=0),
                            ).then_inc(rows_loaded[side][q], 16)

            for side in range(SIDES):
                pool.wait_ge(idx_loaded[side], 16)
                gather(0, side)
            with pool.Fori(1, STEPS) as i:
                for side in range(SIDES):
                    pool.wait_ge(idx_loaded[side], i * 16 + 16)
                    k, count = filled(i - 1, side, len(GROUPS) - 1)
                    pool.wait_ge(bankT_full[k], count)
                    nc.gpsimd.sem_inc(gathers_begun, 1)
                    gather(i, side)

        @block.tensor
        def _(pe):
            def hot_table(i, h):
                lot = LOTS[h // PER_VISIT]
                k, before = visit(i, "hot", 0, h // PER_VISIT)
                if h == lot[0]:
                    wait(pe, bankT_free[k], before)
                if isinstance(i, int) and i == -1:
                    pe.wait_ge(split_ready, h + 1)
                pe.wait_ge(onehot_ready, (i + 1) * HOT + (h + 1))
                o = bankT[k][:, (h - lot[0]) * SB:(h - lot[0] + 1) * SB]
                for c in range(CH[h]):
                    for x in range(2):
                        last = nc.tensor.matmul(o, table[h][x][0:R, c, :], onehot[h % OH][0:R, c, :],
                                                start=c == x == 0, stop=c == CH[h] - 1 and x == 1)
                last.then_inc(onehot_used, 1)

            def hot_rows(i, m):
                for h in LOTS[m]:
                    hot_table(i, h)

            def transpose_group(i, side, q):
                k, before = visit(i, "T", side, q)
                gathered = len([slot for slot in GROUPS[q] if slot])
                pe.wait_ge(rows_loaded[side][q], i * (16 * gathered) + 16 * gathered)
                if q == 0:
                    pe.wait_ge(dense_loaded[side], i * 16 + 16)
                wait(pe, bankT_free[k], before)
                for n, slot in enumerate(GROUPS[q]):
                    last = nc.tensor.transpose(bankT[k][:, n * P:(n + 1) * P], rows[side][:, slot, :], ident[:, :])
                last.then_inc(bankT_full[k], 1)

            def products(i, side, part):
                if part == 0:
                    upto = VISITS.index(("T", side, len(GROUPS) - 1))
                    for k in range(NT):
                        pe.wait_ge(bankT_free[k], i * per_step[k] + (before_loop[k] + BANK[:upto + 1].count(k)))
                x = featT[side]
                for g in range(part * S // 4, (part + 1) * S // 4):
                    for a in range(P // S):
                        at = (a * S + g) * N
                        last = nc.tensor.matmul(gram[a * S:(a + 1) * S, g, 0:N - 1], x[:, at:at + S],
                                                x[:, at + 1:at + N], start=True, stop=True)
                if part == 3:
                    last.then_inc(gram_full, 1)

            def transpose_pairs(i, side):
                pe.wait_ge(pairs_ready, i * SIDES + (side + 1))
                if side:
                    pe.wait_ge(pairsT_ready, i * SIDES + side)
                for c in range(C):
                    last = nc.tensor.transpose(bankZ[:, c * P:(c + 1) * P], pairs[:, c * P:(c + 1) * P], ident[:, :])
                last.then_inc(bankZ_full, 1)

            def three_products(o, weight, value, start, stop):
                nc.tensor.matmul(o, weight[0], value[0], start=start, stop=False)
                nc.tensor.matmul(o, weight[0], value[1], start=False, stop=False)
                return nc.tensor.matmul(o, weight[1], value[0], start=False, stop=stop)

            def layer1(i, m):
                if m == 0:
                    pe.wait_ge(pairsT_ready, i * SIDES + SIDES)
                    pe.wait_ge(denseT_ready, i * SIDES + SIDES)
                if m == M1 // 2:
                    pe.wait_ge(y_taken, i + 1)
                o, w = hidden1_at(m), slice(m * P, (m + 1) * P)
                three_products(o, [wd[x][:, w] for x in range(2)], [denseT[x][:, :] for x in range(2)], True, False)
                for c in range(C):
                    last = three_products(o, [wp[x][:, c, w] for x in range(2)],
                                          [pairsT[x][:, c, :] for x in range(2)], False, c == C - 1)
                if m % 2:
                    last.then_inc(bankH_full[m // 2], 1)

            EARLY = (0, 1)

            def last_bank_free(i, m):
                if m == 1:
                    pe.wait_ge(y_taken, i + 1)
                if m >= 2:
                    k = bankT.index(last_hidden1_bank(m))
                    pe.wait_ge(bankT_free[k], i * per_step[k] + (before_loop[k] + BANK[:SIDES * len(GROUPS)].count(k)))

            def layer1_early(i, m):
                pe.wait_ge(pairsT_ready, i * SIDES + 1)
                pe.wait_ge(denseT_ready, i * SIDES + SIDES)
                last_bank_free(i, m)
                o, w = last_hidden1_at(m), slice(m * P, (m + 1) * P)
                three_products(o, [wd[x][:, w] for x in range(2)], [denseT[x][:, :] for x in range(2)], True, False)
                for c in range(C):
                    three_products(o[:, 0:P], [wp[x][:, c, w] for x in range(2)],
                                   [pairsT[x][:, c, 0:P] for x in range(2)], False, False)

            def layer1_late(i, m):
                w = slice(m * P, (m + 1) * P)
                if m == 0:
                    pe.wait_ge(pairsT_ready, i * SIDES + SIDES)
                if m in EARLY:
                    at = slice(P, SB)
                else:
                    at = slice(0, SB)
                    last_bank_free(i, m)
                    three_products(last_hidden1_at(m), [wd[x][:, w] for x in range(2)],
                                   [denseT[x][:, :] for x in range(2)], True, False)
                for c in range(C):
                    last = three_products(last_hidden1_at(m)[:, at], [wp[x][:, c, w] for x in range(2)],
                                          [pairsT[x][:, c, at] for x in range(2)], False, c == C - 1)
                last.then_inc(last1_full, 1)

            def layer2(i, m):
                o, w = hidden2_at(m), slice(m * P, (m + 1) * P)
                for c in range(M1):
                    if m == 0 and c % 2 == 0:
                        pe.wait_ge(hid1_ready, i * 2 + (c // 2 + 1))
                    last = three_products(o, [w2s[x][:, c, w] for x in range(2)],
                                          [hid1[x][:, c, :] for x in range(2)], c == 0, c == M1 - 1)
                if m == M2 - 1:
                    last.then_inc(bankH_full[0], 1)

            def layer3(i):
                pe.wait_ge(hid2_ready, i + 1)
                for c in range(M2):
                    last = nc.tensor.matmul(bankH[1][0:1, 0:SB], w3s[:, c:c + 1], hid2[:, c, :],
                                            start=c == 0, stop=c == M2 - 1)
                last.then_inc(bankH_full[1], 1)

            def last_layer2():
                for c in range(M1):
                    pe.wait_ge(last1_ready, c + 1)
                    for m in range(M2):
                        last = three_products(last_hidden2_at(m), [w2s[x][:, c, m * P:(m + 1) * P] for x in range(2)],
                                              [hid1[x][:, c, :] for x in range(2)], c == 0, c == M1 - 1)
                        if c == M1 - 1:
                            last.then_inc(last2_full, 1)

            def last_layer3():
                for c in range(M2):
                    pe.wait_ge(last2_ready, c + 1)
                    last = nc.tensor.matmul(bankH[1][0:1, 0:SB], w3s[:, c:c + 1], hid2[:, c, :],
                                            start=c == 0, stop=c == M2 - 1)
                last.then_inc(bankH_full[1], 1)

            def step(i, first=False, last=False):
                def network(layer, *block):
                    if not first:
                        layer(i - 1, *block)

                for q in range(len(GROUPS)):
                    transpose_group(i, 0, q)
                for half in range(2):
                    network(layer1, 2 * half)
                    network(layer1, 2 * half + 1)
                    products(i, 0, 2 * half)
                    products(i, 0, 2 * half + 1)
                for q in range(len(GROUPS) - 1):
                    transpose_group(i, 1, q)
                network(layer2, 0)
                transpose_pairs(i, 0)
                transpose_group(i, 1, len(GROUPS) - 1)
                network(layer2, 1)
                if last:
                    for part in range(4):
                        products(i, 1, part)
                    layer3(i - 1)
                    layer1_early(i, EARLY[0])
                    transpose_pairs(i, 1)
                    layer1_early(i, EARLY[1])
                    for m in range(M1):
                        layer1_late(i, m)
                    last_layer2()
                    last_layer3()
                    return
                for h in LOTS[0]:
                    products(i, 1, 2 * (h - LOTS[0][0]))
                    products(i, 1, 2 * (h - LOTS[0][0]) + 1)
                    hot_table(i, h)
                network(layer3)
                for m in range(1, len(LOTS)):
                    if m == 2:
                        transpose_pairs(i, 1)
                    hot_rows(i, m)

            for side in range(SIDES):
                pe.wait_ge(slack_ready, side + 1)
            pe.wait_ge(ident_ready, 1)
            for m in range(len(LOTS)):
                hot_rows(-1, m)
            step(0, first=True)
            pe.wait_ge(split_ready, WHOLES)
            pe.wait_ge(small_loaded, 3 * 16)
            with pe.Fori(1, STEPS - 1) as i:
                step(i)
            step(STEPS - 1, last=True)

        def copy_group(i, eng, copy, side, q):
            k, count = filled(i, side, q)
            eng.wait_ge(bankT_full[k], count)
            group = GROUPS[q]
            src = bankT[k][:, 0:len(group) * P].rearrange("p (n b) -> p n b", b=P)
            dst = by_sample(side)[:, :, group[0]:group[-1] + 1].rearrange("p b n -> p n b")
            copy(dst, src).then_inc(bankT_free[k], 1)

        @block.scalar
        def _(act):
            nc.scalar.sem_inc(y_taken, 1)

            def high(n):
                _, place, whole, parts = SPLITS[n]
                act.wait_ge(staged[place], user_of_place(n)[0] * 16)
                if n == WHOLES - 1:
                    act.wait_ge(wd_summed, 1)
                    whole = wd_whole[:, 0, :]
                nc.scalar.copy(parts[0], whole).then_inc(high_ready, 1)

            def copy_hot(i, m):
                k, _ = visit(i, "hot", 0, m)
                act.wait_ge(onehot_used, (i + 1) * HOT + (LOTS[m][-1] + 1))
                lot, first = LOTS[m], NC + LOTS[m][0]
                src = bankT[k][:, 0:len(lot) * SB].rearrange("p (n s b) -> p n s b", s=SIDES, b=P)
                for side in range(SIDES):
                    last = nc.scalar.copy(by_sample(side)[:, :, first:first + len(lot)].rearrange("p b n -> p n b"),
                                          src[:, :, side, :])
                last.then_inc(bankT_free[k], 1)

            def pairs_high(i, side):
                act.wait_ge(bankZ_full, i * SIDES + (side + 1))
                nc.scalar.copy(pairsT[0][:, :, side * P:(side + 1) * P],
                               bankZ[:, 0:C * P].rearrange("p (c b) -> p c b", b=P)).then_inc(pairsT_high_ready, 1)

            def hidden1(i):
                for half in range(2):
                    act.wait_ge(bankH_full[half], i * 2 + 1)
                    for m in (2 * half, 2 * half + 1):
                        last = nc.scalar.activation(hid1_whole[:, m, :], hidden1_at(m),
                                                    ACT.Relu, bias=b1s[:, m:m + 1])
                    last.then_inc(hid1_full, 1)

            def hidden2(i):
                act.wait_ge(bankH_full[0], i * 2 + 2)
                for m in range(M2):
                    last = nc.scalar.activation(hid2[:, m, :], hidden2_at(m),
                                                ACT.Relu, bias=b2s[:, m:m + 1])
                last.then_inc(hid2_ready, 1)

            def result(i):
                act.wait_ge(bankH_full[1], i * 2 + 2)
                nc.scalar.copy(y_row[:, bass.ds(i * SB, SB)], bankH[1][0:1, 0:SB]).then_inc(y_taken, 1)

            def step(i, first=False, last=False):
                for q in range(len(GROUPS)):
                    if on_scalar(q):
                        copy_group(i, act, nc.scalar.copy, 0, q)
                if first:
                    high(WHOLES - 1)
                else:
                    hidden1(i - 1)
                for q in range(len(GROUPS) - 1):
                    copy_group(i, act, nc.scalar.copy, 1, q)
                pairs_high(i, 0)
                copy_group(i, act, nc.scalar.copy, 1, len(GROUPS) - 1)
                if not first:
                    hidden2(i - 1)
                if last:
                    result(i - 1)
                    pairs_high(i, 1)
                    return
                if not first:
                    result(i - 1)
                for m in range(len(LOTS)):
                    if m == 2:
                        pairs_high(i, 1)
                    copy_hot(i, m)

            for h in range(HOT):
                high(h)
                if h >= AHEAD and (h - AHEAD) % PER_VISIT == PER_VISIT - 1:
                    copy_hot(-1, (h - AHEAD) // PER_VISIT)
                    copied = (h - AHEAD) // PER_VISIT + 1
            for n in range(HOT, WHOLES - 1):
                high(n)
            for m in range(copied, len(LOTS)):
                copy_hot(-1, m)
            act.wait_ge(small_loaded, 3 * 16)
            step(0, first=True)
            with act.Fori(1, STEPS - 1) as i:
                step(i)
            step(STEPS - 1, last=True)
            for m in range(M1):
                act.wait_ge(last1_full, m + 1)
                nc.scalar.activation(hid1_whole[:, m, :], last_hidden1_at(m), ACT.Relu, bias=b1s[:, m:m + 1])\
                  .then_inc(last1_whole, 1)
            for m in range(M2):
                act.wait_ge(last2_full, m + 1)
                nc.scalar.activation(hid2[:, m, :], last_hidden2_at(m), ACT.Relu, bias=b2s[:, m:m + 1])\
                  .then_inc(last2_ready, 1)
            act.wait_ge(bankH_full[1], STEPS * 2 - 1)
            nc.scalar.copy(y_row[:, (STEPS - 1) * SB:B], bankH[1][0:1, 0:SB]).then_inc(y_taken, 1)

        @block.vector
        def _(dve):
            def low(n):
                _, _, whole, parts = SPLITS[n]
                if n == WHOLES - 1:
                    whole = wd_whole[:, 0, :]
                dve.wait_ge(high_ready, n + 1)
                nc.vector.tensor_tensor(parts[1], whole, parts[0].bitcast(fp32), ALU.subtract)\
                  .then_inc(split_ready, 1)

            def onehots(i, h):
                if not isinstance(i, int) or i >= 0:
                    if h == 0:
                        dve.wait_ge(ids_wide_loaded, i * 16 + 32)
                elif h == 0:
                    dve.wait_ge(first_ids_loaded, 16)
                elif h == 1:
                    dve.wait_ge(ids_wide_loaded, 16)
                wait(dve, onehot_used, (i + 1) * HOT + (h - OH + 1))
                for c in range(CH[h]):
                    last = nc.vector.tensor_scalar(onehot[h % OH][0:R, c, :], ids_wide[0:R, h, :],
                                                   row_no[0:R, c:c + 1], None, ALU.is_equal)
                last.then_inc(onehot_ready, 1)

            def dense_parts_of(i, side):
                k, before = visit(i, "T", side, 0)
                dve.wait_ge(bankT_free[k], before + 1)
                source, mine = by_sample(side)[:, :, 0], slice(side * P, (side + 1) * P)
                nc.vector.tensor_copy(denseT[0][:, mine], source).then_inc(dense_high_ready, 1)
                dve.wait_ge(dense_high_ready, i * SIDES + (side + 1))
                nc.vector.tensor_tensor(denseT[1][:, mine], source, denseT[0][:, mine].bitcast(fp32),
                                        ALU.subtract).then_inc(denseT_ready, 1)

            def triangle(i, side):
                dve.wait_ge(gram_full, i * SIDES + (side + 1))
                nc.vector.transpose(square[:, :, :], gram[:, :, 0:N - 1].rearrange("p g j -> p j g"))\
                  .then_inc(square_ready, 1)
                dve.wait_ge(square_ready, i * SIDES + (side + 1))
                for j0, j1, at in RECTANGLES:
                    width = j1 - 1
                    last = nc.vector.tensor_copy(
                        pairs[:, at:at + (j1 - j0) * width].rearrange("p (j i) -> p j i", i=width),
                        square[:, j0 - 1:j1 - 1, 0:width])
                last.then_inc(pairs_ready, 1)

            def pairs_low(i, side):
                dve.wait_ge(pairsT_high_ready, i * SIDES + (side + 1))
                mine = slice(side * P, (side + 1) * P)
                nc.vector.tensor_tensor(pairsT[1][:, :, mine], bankZ[:, 0:C * P].rearrange("p (c b) -> p c b", b=P),
                                        pairsT[0][:, :, mine].bitcast(fp32), ALU.subtract).then_inc(pairsT_ready, 1)

            def split_hidden1(i):
                for half in range(2):
                    dve.wait_ge(hid1_full, i * 2 + (half + 1))
                    whole, *parts = [t[:, 2 * half:2 * half + 2, :] for t in (hid1_whole, *hid1)]
                    nc.vector.tensor_copy(parts[0], whole).then_inc(hid1_high_ready, 1)
                    dve.wait_ge(hid1_high_ready, i * 2 + (half + 1))
                    nc.vector.tensor_tensor(parts[1], whole, parts[0].bitcast(fp32), ALU.subtract)\
                      .then_inc(hid1_ready, 1)

            def dense_weights_low():
                dve.wait_ge(staged[SPLITS[-1][1]], user_of_place(WHOLES - 1)[0] * 16)
                nc.vector.tensor_tensor(wd_whole[:, 0, :], wd_whole[:, 0, :], wd_whole[:, 1, :], ALU.add)\
                  .then_inc(wd_summed, 1)
                low(WHOLES - 1)

            def step(i, first=False, last=False):
                def make(*which):
                    if not last:
                        for h in which:
                            onehots(i, h)

                for q in range(len(GROUPS)):
                    if not on_scalar(q):
                        copy_group(i, dve, nc.vector.tensor_copy, 0, q)
                if first:
                    dense_weights_low()
                    make(0)
                else:
                    make(*range(OH))
                    split_hidden1(i - 1)
                triangle(i, 0)
                for side in range(SIDES):
                    dense_parts_of(i, side)
                pairs_low(i, 0)
                if first:
                    make(*range(1, OH))
                make(OH)
                triangle(i, 1)
                make(*range(OH + 1, HOT))
                pairs_low(i, 1)

            for side in range(SIDES):
                nc.vector.memset(featT[side][:, P * N:P * N + S], 0.0).then_inc(slack_ready, 1)
            dve.wait_ge(row_no_counted, 1)
            nc.vector.tensor_copy(row_no[:, :], row_no_int[:, :]).then_inc(row_no_ready, 1)
            dve.wait_ge(row_no_ready, 1)
            for h in range(HOT):
                onehots(-1, h)
                low(h)
            for n in range(HOT, WHOLES - 1):
                low(n)
            step(0, first=True)
            with dve.Fori(1, STEPS - 1) as i:
                step(i)
            step(STEPS - 1, last=True)
            for m in range(M1):
                dve.wait_ge(last1_whole, m + 1)
                nc.vector.tensor_copy(hid1[0][:, m, :], hid1_whole[:, m, :]).then_inc(last1_high, 1)
                dve.wait_ge(last1_high, m + 1)
                nc.vector.tensor_tensor(hid1[1][:, m, :], hid1_whole[:, m, :], hid1[0][:, m, :].bitcast(fp32),
                                        ALU.subtract).then_inc(last1_ready, 1)


N_TABLES = 26
N_HOT = 8


def kernel(**inputs):
    import numpy as _np
    import concourse.bacc as _bacc
    from concourse import mybir as _mybir
    from concourse.bass_utils import run_bass_kernel_spmd as _run

    dense, ids = _np.asarray(inputs["r_dense_features"]), _np.asarray(inputs["ids"])
    tables = [_np.asarray(inputs[f"tbl_{f}"]) for f in range(N_TABLES)]
    w1, w2, w3 = (_np.asarray(inputs[n]) for n in ("W_top1", "W_top2", "W_top3"))
    d, n, h1, h2 = dense.shape[1], N_TABLES + 1, w1.shape[1], w2.shape[1]

    by_size = sorted(range(N_TABLES), key=lambda f: len(tables[f]))
    hot, cold = by_size[:N_HOT], sorted(by_size[N_HOT:])
    hot.insert(1, hot.pop())
    feature = [0] + [1 + f for f in cold + hot]

    found, places = rectangles(n)
    w_pairs = _np.zeros((places, h1), w1.dtype)
    row = {}
    for i in range(n):
        for j in range(i + 1, n):
            row[i, j] = d + len(row)
    for j0, j1, at in found:
        for j in range(j0, j1):
            for i in range(j):
                pair = tuple(sorted((feature[i], feature[j])))
                w_pairs[at + (j - j0) * (j1 - 1) + i] = w1[row[pair]]
    w_pairs = w_pairs.reshape(-1, P, h1).transpose(1, 0, 2)
    w_dense = _np.stack([w1[0:d], w1[d + len(row):]], axis=1)

    arrays = {
        "cold_ids": ids[:, cold], "hot_ids": ids[:, hot].T, "dense": dense,
        **{f"tbl_{f}": tables[f] for f in range(N_TABLES)},
        "w_dense": w_dense, "w_pairs": w_pairs,
        "b1": _np.asarray(inputs["b_top1"]).reshape(-1, P).T,
        "w2": w2.reshape(-1, P, h2).transpose(1, 0, 2),
        "b2": _np.asarray(inputs["b_top2"]).reshape(-1, P).T,
        "w3": w3.reshape(-1, P).T,
    }
    nc = _bacc.Bacc("TRN2", target_bir_lowering=False, num_devices=1)
    given = {k: _np.ascontiguousarray(a) for k, a in arrays.items()}
    ap = {k: nc.dram_tensor(f"in_{k}", a.shape, _mybir.dt.from_np(a.dtype), kind="ExternalInput").ap()
          for k, a in given.items()}
    out = nc.dram_tensor("out_y", (dense.shape[0], 1), _mybir.dt.float32, kind="ExternalOutput").ap()
    dlrm_tower(nc, ap["cold_ids"], ap["hot_ids"], ap["dense"], [ap[f"tbl_{f}"] for f in cold],
               [ap[f"tbl_{f}"] for f in hot], ap["w_dense"], ap["w_pairs"],
               ap["b1"], ap["w2"], ap["b2"], ap["w3"], out)
    r = _run(nc, [{f"in_{k}": a for k, a in given.items()}], core_ids=[0])
    return r.results[0]["out_y"]
```
